# Optimizing a Trainium2 kernel written in Bass

```python
import numpy as np
import jax
import jax.numpy as jnp

def _softmax(x, axis=-1):
    return jax.nn.softmax(x, axis=axis)

def _gelu(x):
    return jax.nn.gelu(x, approximate=True)

def _silu(x):
    return jax.nn.silu(x)

def _sigmoid(x):
    return jax.nn.sigmoid(x)

def _layernorm(x, axis=-1, eps=1e-05):
    m = jnp.mean(x, axis=axis, keepdims=True)
    v = jnp.var(x, axis=axis, keepdims=True)
    return (x - m) / jnp.sqrt(v + eps)

def _scatter_add(tgt, idx, src, axis=0):
    return tgt.at[idx].add(src)

def _segment_sum(src, seg, n):
    return jax.ops.segment_sum(src, seg, n)
kernel_name = 'mk_cond_resid_d2_seqx_r2_8d22db'

def setup_inputs(seed: int=0):
    np.random.seed(seed)
    _w = jnp.asarray

    def _rec_inputs():
        import jax
        import jax.numpy as jnp
        _rk = jax.random.key(seed)
        x = -0.000125 + 0.9999 * jax.random.normal(jax.random.fold_in(_rk, 1), (64, 128, 2048), jnp.float32)
        _lenS = 128 - jax.random.randint(jax.random.fold_in(_rk, 7), (64,), 0, max(1, 128 // 4) + 1, jnp.int32)
        _lenS2 = 128 - jax.random.randint(jax.random.fold_in(_rk, 8), (64,), 0, max(1, 128 // 4) + 1, jnp.int32)
        cond_128 = 0.0061147 + 1.02565 * jax.random.normal(jax.random.fold_in(_rk, 11), (64, 128), jnp.float32)
        fside_S_0 = -0.022604 + 0.987366 * jax.random.normal(jax.random.fold_in(_rk, 12), (128,), jnp.float32)
        return (x, cond_128, fside_S_0)
    x, cond_128, fside_S_0 = _rec_inputs()

    def _L0_cond_setup():
        import jax, jax.numpy as jnp
        import numpy as np
        from jax import lax
        N, C_IN, L = (32, 128, 2048)
        C_OUT, K, GROUPS = (128, 9, 4)
        C_DIM, PAD, STRIDE = (128, 4, 1)
        key = jax.random.key(seed)
        k1, k2, k3, k4, k5 = jax.random.split(key, 5)
        x = jax.random.normal(k1, (N, C_IN, L), dtype=jnp.float32)
        c = jax.random.normal(k2, (N, C_DIM), dtype=jnp.float32)
        weight = jax.random.normal(k3, (C_OUT, C_IN // GROUPS, K), dtype=jnp.float32)
        c_weight = jax.random.normal(k4, (C_OUT, C_DIM), dtype=jnp.float32)
        bias = jax.random.normal(k5, (C_OUT,), dtype=jnp.float32)
        return {'x': x, 'c': c, 'weight': weight, 'c_weight': c_weight, 'bias': bias}
    _L0_cond_all = _L0_cond_setup()
    _L0_cond_in = {k: v for k, v in _L0_cond_all.items() if k in ('weight', 'c_weight')}
    del _L0_cond_all

    def _L1_cond_setup():
        import jax, jax.numpy as jnp
        import numpy as np
        K = 8
        T = 1.0
        D_EMBD = 128
        IN_C = 128
        OUT_C = 128
        BS = 32
        H = 2048
        HID = 128
        key = jax.random.key(seed)
        ks = jax.random.split(key, 10)
        s = lambda fan_in: 1.0 / np.sqrt(fan_in)
        return {'x': jax.random.normal(ks[0], (BS, IN_C, H), dtype=jnp.float32), 'embedding': jax.random.normal(ks[1], (BS, D_EMBD), dtype=jnp.float32), 'W0': jax.random.normal(ks[2], (D_EMBD, HID), dtype=jnp.float32) * s(D_EMBD), 'b0': jnp.zeros((HID,), dtype=jnp.float32), 'W1': jax.random.normal(ks[3], (HID, HID), dtype=jnp.float32) * s(HID), 'b1': jnp.zeros((HID,), dtype=jnp.float32), 'W2': jax.random.normal(ks[4], (HID, K), dtype=jnp.float32) * s(HID), 'b2': jnp.zeros((K,), dtype=jnp.float32), 'weight': jax.random.normal(ks[5], (K, OUT_C, IN_C, 1), dtype=jnp.float32) * s(IN_C), 'bias_k': jax.random.normal(ks[6], (K, OUT_C), dtype=jnp.float32) * 0.1}
    _L1_cond_all = _L1_cond_setup()
    _L1_cond_in = {k: v for k, v in _L1_cond_all.items() if k in ('W0', 'b0', 'W1', 'b1', 'W2', 'b2', 'weight', 'bias_k')}
    del _L1_cond_all
    return {'x': x, 'cond_128': cond_128, 'fside_S_0': fside_S_0, 'L0_cond_weight': _L0_cond_in['weight'], 'L0_cond_c_weight': _L0_cond_in['c_weight'], 'L1_cond_W0': _L1_cond_in['W0'], 'L1_cond_b0': _L1_cond_in['b0'], 'L1_cond_W1': _L1_cond_in['W1'], 'L1_cond_b1': _L1_cond_in['b1'], 'L1_cond_W2': _L1_cond_in['W2'], 'L1_cond_b2': _L1_cond_in['b2'], 'L1_cond_weight': _L1_cond_in['weight'], 'L1_cond_bias_k': _L1_cond_in['bias_k']}

def reference(x, cond_128, fside_S_0, L0_cond_weight, L0_cond_c_weight, L1_cond_W0, L1_cond_b0, L1_cond_W1, L1_cond_b1, L1_cond_W2, L1_cond_b2, L1_cond_weight, L1_cond_bias_k):
    import jax
    import jax.numpy as jnp

    def _L0_cond_ref(x, c, weight, c_weight, bias):
        import jax, jax.numpy as jnp
        import numpy as np
        from jax import lax
        N, C_IN, L = (32, 128, 2048)
        C_OUT, K, GROUPS = (128, 9, 4)
        C_DIM, PAD, STRIDE = (128, 4, 1)
        out = lax.conv_general_dilated(x, weight, window_strides=(STRIDE,), padding=[(PAD, PAD)], dimension_numbers=('NCH', 'OIH', 'NCH'), feature_group_count=GROUPS)
        ctx = jnp.einsum('nd,od->no', c, c_weight)
        out = out + ctx[:, :, None] + bias[None, :, None]
        return out

    def _L1_cond_ref(x, embedding, W0, b0, W1, b1, W2, b2, weight, bias_k):
        import jax, jax.numpy as jnp
        import numpy as np
        K = 8
        T = 1.0
        D_EMBD = 128
        IN_C = 128
        OUT_C = 128
        BS = 32
        H = 2048
        HID = 128
        h = jax.nn.gelu(embedding @ W0 + b0, approximate=False)
        h = jax.nn.gelu(h @ W1 + b1, approximate=False)
        att = jax.nn.softmax((h @ W2 + b2) / T, axis=-1)
        agg_w = jnp.einsum('bk,koi->boi', att, weight[..., 0])
        agg_b = att @ bias_k
        out = jnp.einsum('boi,bih->boh', agg_w, x) + agg_b[:, :, None]
        return out
    x = x + _L0_cond_ref(x, cond_128, L0_cond_weight, L0_cond_c_weight, fside_S_0)
    x = x + _L1_cond_ref(x, cond_128, L1_cond_W0, L1_cond_b0, L1_cond_W1, L1_cond_b1, L1_cond_W2, L1_cond_b2, L1_cond_weight, L1_cond_bias_k)
    return x

_drawn_inputs = setup_inputs


def setup_inputs(seed=0):
    import zlib

    import numpy as np

    out = dict(_drawn_inputs(seed))
    spreads = {'L1_cond_b0': (0.0, 0.627), 'L1_cond_b1': (0.0, 0.436), 'L1_cond_b2': (0.0, 0.348)}
    factors = {'L1_cond_bias_k': 33.446}
    for name, (base, spread) in spreads.items():
        noise = np.random.default_rng([zlib.crc32(name.encode()), seed]).standard_normal(out[name].shape)
        drawn = base * np.exp(spread * noise) if base else spread * noise
        out[name] = jnp.asarray(drawn.astype(out[name].dtype))
    for name, factor in factors.items():
        out[name] = (out[name] * factor).astype(out[name].dtype)
    return out
```

```python
from contextlib import ExitStack

import concourse.bass as bass
from concourse import mybir

F32 = mybir.dt.float32
F32R = mybir.dt.float32r
ALU = mybir.AluOpType
ACT = mybir.ActivationFunctionType
AX = mybir.AxisListType

P = 128
PH = 4
U = 4
Q = 32
DMA = 16
AHEAD = 7
ACT_PHASES = 1


def after(sample, lag):
    n, k = sample
    return n + (k + lag) // U, (k + lag) % U


def number(sample):
    n, k = sample
    return n * U + k


def done(sample, each=1, lag=0):
    n, k = sample
    return n * (U * each) + (k + 1 + lag) * each


def buf(sample):
    return sample[1] % 2


def uses(sample):
    n, k = sample
    return n * (U // 2) + k // 2


def pair_buf(sample):
    return sample[1] // 2


def at_least(eng, sem, value):
    if isinstance(value, int) and value <= 0:
        return
    eng.wait_ge(sem, value)


def cond_resid_kernel(nc, x, cond, bias, conv_w, ctx_w, w0, b0, w1, b1, w2, b2, mix_w, mix_b, out):
    NS, C, T = x.shape
    CG, K = conv_w.shape[1:]
    G = C // CG
    NK = mix_b.shape[0]
    N = T // PH
    PAD = K // 2
    ROUNDS = NS // U
    PC = NK + 2
    assert C == P and CG == Q and G == PH and N == 512 and K <= 2 * PH + 1 and NS % U == 0

    with ExitStack() as stack:
        def sb(name, shape, dt=F32):
            return stack.enter_context(nc.sbuf_tensor(name, shape, dt))

        def sem(name):
            return stack.enter_context(nc.semaphore(name))

        def two(make, name, *args):
            return [make(f"{name}{k}", *args) for k in range(2)]

        x_in = two(sb, "x_in", [P, T])
        x_ph = two(sb, "x_ph", [P, PH, 2, N])
        x_cv = two(sb, "x_cv", [P, G, 2, N])
        x_hi = two(sb, "x_hi", [P, G, N + 2], F32R)
        x_lo = two(sb, "x_lo", [P, G, N + 2], F32R)
        y_st = two(sb, "y_st", [P, N])
        y_in = two(sb, "y_in", [P, PH, N])
        y_hi = sb("y_hi", [P, PH, N], F32R)
        y_lo = sb("y_lo", [P, PH, N], F32R)
        z_out = two(sb, "z_out", [P, T])
        par = two(sb, "par", [P, PC])
        mix_prod = sb("mix_prod", [P, NK, P])
        mix_sum_f = sb("mix_sum_f", [P, P])
        mix_f = sb("mix_f", [P, P])
        mix_hi = two(sb, "mix_hi", [P, P], F32R)
        mix_lo = two(sb, "mix_lo", [P, P], F32R)

        cw_hi = sb("cw_hi", [P, G, 3, P], F32R)
        cw_lo = sb("cw_lo", [P, G, 3, P], F32R)
        cw_f = z_out[0][:, 0:G * 3 * P].rearrange("p (g b o) -> p g b o", g=G, b=3)
        cw_rep = z_out[1][:, 0:K * P].rearrange("o (k q c) -> o k q c", k=K, q=PH)
        cw_nat = z_out[1][:, K * P:K * P + CG * K].rearrange("o (c k) -> o c k", k=K)
        ctxw_nat = sb("ctxw_nat", [P, P])
        cond_nat = sb("cond_nat", [NS, P])
        cond_t = sb("cond_t", [P, NS])
        ctxw_t = sb("ctxw_t", [P, P])
        w0_sb = sb("w0_sb", [P, P])
        w1_sb = sb("w1_sb", [P, P])
        w2_sb = sb("w2_sb", [P, NK])
        b2_sb = sb("b2_sb", [1, NK])
        cols = sb("cols", [P, 3])
        mixb_sb = sb("mixb_sb", [NK, P])
        mixw_nat = y_in[0][:, 0:2, :].rearrange("o q n -> o (q n)").rearrange("o (k i) -> o k i", k=NK)
        mixw_t = sb("mixw_t", [P, NK, P])
        h1 = sb("h1", [P, NS])
        h2 = sb("h2", [P, NS])
        ident = sb("ident", [P, P])
        ones = sb("ones", [NS, P])
        logit = sb("logit", [NS, NK])
        top = sb("top", [NS, 1])
        ntop = sb("ntop", [NS, 1])
        expd = sb("expd", [NS, NK])
        total = sb("total", [NS, 1])
        inv = sb("inv", [NS, 1])
        att = sb("att", [NS, NK])
        att_t = sb("att_t", [NK, NS])
        att_diag = sb("att_diag", [NS, NS, NK])
        table = sb("table", [P, NS, PC])

        ps = stack.enter_context(nc.psum_tensor("ps", [P, 8, 512], F32))
        y_ps = ps[:, 0:G, :]
        z_ps = ps[:, G:G + PH, :]

        weights_loaded = sem("weights_loaded")
        conv_w_loaded = sem("conv_w_loaded")
        ident_made = sem("ident_made")
        consts_made = sem("consts_made")
        cw_cleared = sem("cw_cleared")
        halos_cleared = sem("halos_cleared")
        taps_spread = sem("taps_spread")
        taps_turned = sem("taps_turned")
        taps_placed_act = sem("taps_placed_act")
        taps_placed_dve = sem("taps_placed_dve")
        conv_w_ready = sem("conv_w_ready")
        cond_turned = sem("cond_turned")
        cond_copied = sem("cond_copied")
        mixw_turned = sem("mixw_turned")
        mixw_copied = sem("mixw_copied")
        mlp_mm = sem("mlp_mm")
        mlp_act = sem("mlp_act")
        soft = sem("soft")
        ctx_mm = sem("ctx_mm")
        aggb_mm = sem("aggb_mm")
        att_mm = sem("att_mm")
        table_made = sem("table_made")

        x_loaded = two(sem, "x_loaded")
        x_split_ph = sem("x_split_ph")
        x_moved = two(sem, "x_moved")
        x_hi_made = sem("x_hi_made")
        x_lo_made = sem("x_lo_made")
        y_ready = sem("y_ready")
        y_out_act = sem("y_out_act")
        y_out_dve = sem("y_out_dve")
        y_moved = two(sem, "y_moved")
        y_hi_made = sem("y_hi_made")
        y_lo_made = sem("y_lo_made")
        par_made = sem("par_made")
        prod_made = sem("prod_made")
        mix_sum = sem("mix_sum")
        mix_hi_made = sem("mix_hi_made")
        mix_made = sem("mix_made")
        z_ready = sem("z_ready")
        z_read = sem("z_read")
        z_stored = two(sem, "z_stored")

        def exists(sample):
            n, _ = sample
            return not isinstance(n, int) or 0 <= n < ROUNDS

        def pipeline(eng, slot):
            last = ROUNDS - (AHEAD + U - 1) // U
            for k in range(U):
                slot((0, k))
            with eng.Fori(1, last) as n:
                for k in range(U):
                    slot((n, k))
            for s in range(U * last, NS + 2):
                slot((s // U, s % U))

        block = stack.enter_context(nc.Block())

        @block.sync
        def _(sp):
            def ahead(*values):
                for v in values:
                    if not isinstance(v, int):
                        sp.compute_val(v)
                return values

            def load(s):
                if not exists(s):
                    return
                b, split = ahead(number(s), done(s, lag=-2))
                at_least(sp, x_split_ph, split)
                sp.dma_start(x_in[buf(s)][:, :], x[b, :, :]).then_inc(x_loaded[buf(s)], DMA)

            def move_x(s, phases):
                if not exists(s):
                    return
                b = pair_buf(s)
                split, low = ahead(done(s, lag=1), done(s, lag=-3))
                sp.wait_ge(x_split_ph, split)
                at_least(sp, x_lo_made, low)
                for p in phases:
                    for g in range(G):
                        sp.dma_start(x_cv[b][Q * p:Q * p + Q, g, :, :],
                                     x_ph[b][Q * g:Q * g + Q, p, :, :]).then_inc(x_moved[b], DMA)

            def move_y(s):
                if not exists(s):
                    return
                taken, low = ahead(done(s, G, lag=-1) + 1, done(s, lag=-2))
                sp.wait_ge(y_out_act, taken)
                at_least(sp, y_lo_made, low)
                for r in range(PH):
                    sp.dma_start(y_in[buf(s)][0:Q, r, :],
                                 y_st[buf(s)][Q * r:Q * r + Q, :]).then_inc(y_moved[buf(s)], DMA)

            def store(s):
                if not exists(s):
                    return
                b, read = ahead(number(s), done(s))
                sp.wait_ge(z_read, read)
                sp.dma_start(out[b, :, :], z_out[buf(s)][:, :]).then_inc(z_stored[buf(s)], DMA)

            sp.dma_start(cw_nat[:, :, :], conv_w[:, :, :]).then_inc(conv_w_loaded, DMA)
            load((0, 0))
            load((0, 1))
            for to, of in (
                (cond_nat[:, :], cond[:, :]),
                (ctxw_nat[:, :], ctx_w[:, :]),
                (w0_sb[:, :], w0[:, :]),
                (w1_sb[:, :], w1[:, :]),
                (w2_sb[:, :], w2[:, :]),
                (b2_sb[:, :], b2.rearrange("(a k) -> a k", a=1)),
                (cols[:, 0:1], bias.rearrange("(c a) -> c a", a=1)),
                (cols[:, 1:2], b0.rearrange("(c a) -> c a", a=1)),
                (cols[:, 2:3], b1.rearrange("(c a) -> c a", a=1)),
                (mixb_sb[:, :], mix_b[:, :]),
                (mixw_nat[:, :, :], mix_w.rearrange("k o i a -> o k (i a)")),
            ):
                sp.dma_start(to, of).then_inc(weights_loaded, DMA)
            load((0, 2))
            load((0, 3))
            move_x((0, 0), range(PH))
            for k in range(4, AHEAD):
                load(after((0, 0), k))
            move_x((0, 2), range(0, 2))

            def slot(s):
                store(after(s, -2))
                move_y(s)
                if s[1] % 2:
                    move_x(after(s, 3), range(0, 2))
                else:
                    move_x(after(s, 2), range(2, PH))
                load(after(s, AHEAD))

            pipeline(sp, slot)
            for k in range(2):
                sp.wait_ge(z_stored[k], DMA * (NS // 2))

        @block.tensor
        def _(pe):
            pe.wait_ge(ident_made, 2)
            pe.wait_ge(taps_spread, 1)
            for k in range(K):
                mm = pe.transpose(ps[:, k // 4, k % 4 * P:k % 4 * P + P],
                                  cw_rep[:, k, :, :].rearrange("o q c -> o (q c)"), ident[:, :])
            mm.then_inc(taps_turned, 1)
            pe.wait_ge(weights_loaded, DMA * 11)
            pe.transpose(ps[:, 3, 0:NS], cond_nat[:, :], ident[0:NS, 0:NS])
            pe.transpose(ps[:, 3, P:2 * P], ctxw_nat[:, :], ident[:, :]).then_inc(cond_turned, 1)
            for k in range(NK):
                mm = pe.transpose(ps[:, 4 + k // 4, k % 4 * P:k % 4 * P + P], mixw_nat[:, k, :], ident[:, :])
            mm.then_inc(mixw_turned, 1)
            pe.wait_ge(cond_copied, 2)
            pe.matmul(ps[:, 6, 0:NS], w0_sb[:, :], cond_t[:, :], start=True, stop=True).then_inc(mlp_mm, 1)
            pe.matmul(ps[:, 3, 0:NS], ctxw_t[:, :], cond_t[:, :], start=True, stop=True).then_inc(ctx_mm, 1)
            pe.wait_ge(mlp_act, 1)
            pe.matmul(ps[:, 7, 0:NS], w1_sb[:, :], h1[:, :], start=True, stop=True).then_inc(mlp_mm, 1)
            pe.wait_ge(mlp_act, 2)
            pe.wait_ge(consts_made, 1)
            pe.matmul(ps[0:NS, 6, 0:NK], h2[:, :], w2_sb[:, :], start=True, stop=False)
            pe.matmul(ps[0:NS, 6, 0:NK], ones[0:1, 0:NS], b2_sb[:, :], start=False, stop=True).then_inc(mlp_mm, 1)

            def attention():
                pe.wait_ge(soft, 6)
                pe.transpose(ps[0:NK, 7, 0:NS], att[:, :], ident[0:NS, 0:NS]).then_inc(att_mm, 1)
                pe.wait_ge(soft, 8)
                pe.matmul(ps[:, 6, 0:NS], mixb_sb[:, :], att_t[:, :], start=True, stop=True).then_inc(aggb_mm, 1)
                pe.matmul(ps[:, 7, :], ones[:, :], att_diag[:, :, :].rearrange("p s k -> p (s k)"),
                          start=True, stop=True).then_inc(att_mm, 1)

            def conv(s):
                if not exists(s):
                    return
                pe.wait_ge(x_lo_made, done(s))
                for g in range(G):
                    at_least(pe, y_out_act, done(s, G, lag=-2) + g + 1)
                    if g == G - 1:
                        at_least(pe, y_out_dve, done(s, lag=-1))
                    terms = [(w, xx, b) for w, xx in ((cw_hi, x_hi), (cw_lo, x_hi), (cw_hi, x_lo)) for b in range(3)]
                    for n, (w, xx, b) in enumerate(terms):
                        mm = pe.matmul(y_ps[:, g, :], w[:, g, b, :], xx[buf(s)][:, g, b:b + N],
                                       start=n == 0, stop=n == len(terms) - 1)
                    mm.then_inc(y_ready, 1)

            def mix(s):
                if not exists(s):
                    return
                pe.wait_ge(y_lo_made, done(s))
                pe.wait_ge(mix_made, done(s))
                at_least(pe, z_read, done(s, lag=-1))
                for r in range(PH):
                    terms = [(mix_hi, y_hi), (mix_lo, y_hi), (mix_hi, y_lo)]
                    for n, (w, yy) in enumerate(terms):
                        mm = pe.matmul(z_ps[:, r, :], w[buf(s)][:, :], yy[:, r, :],
                                       start=n == 0, stop=n == len(terms) - 1)
                mm.then_inc(z_ready, 1)

            def slot(s):
                conv(s)
                if isinstance(s[0], int) and number(s) == 0:
                    attention()
                    pe.wait_ge(table_made, 3)
                mix(after(s, -1))

            pe.wait_ge(conv_w_ready, 2)
            pe.wait_ge(halos_cleared, 4)
            pe.wait_ge(table_made, 1)
            pipeline(pe, slot)

        def place(k, q):
            r = (q - k) % PH
            return r, (k - PAD + r - q) // PH + 1

        def put_taps(eng, phases, write, placed):
            eng.wait_ge(taps_turned, 1)
            eng.wait_ge(cw_cleared, 1)
            for q in phases:
                for k in range(K):
                    r, b = place(k, q)
                    n = write(cw_f[Q * q:Q * q + Q, :, b, Q * r:Q * r + Q],
                              ps[Q * q:Q * q + Q, k // 4, k % 4 * P:k % 4 * P + P].rearrange("c (g o) -> c g o", g=G))
            n.then_inc(placed, 1)

        @block.scalar
        def _(act):
            def split_phases(s):
                if not exists(s):
                    return
                act.wait_ge(x_loaded[buf(s)], DMA * (uses(s) + 1))
                at_least(act, x_moved[pair_buf(s)], DMA * PH * G * s[0])
                nc.scalar.activation(x_ph[pair_buf(s)][:, :, buf(s), :], x_in[buf(s)][:, :].rearrange("c (n q) -> c q n", q=PH),
                                     ACT.Copy).then_inc(x_split_ph, 1)

            def take_y(s, g):
                if not exists(s):
                    return
                act.wait_ge(y_ready, done(s, G, lag=-1) + g + 1)
                if g == 0:
                    at_least(act, y_moved[buf(s)], DMA * PH * uses(s))
                    nc.scalar.activation(y_st[buf(s)][:, :], y_ps[:, 0, :], ACT.Copy).then_inc(y_out_act, 1)
                    return
                if g == 1:
                    at_least(act, y_lo_made, done(s, lag=-2))
                for r in range(ACT_PHASES if g == G - 1 else PH):
                    n = nc.scalar.activation(y_in[buf(s)][Q * g:Q * g + Q, r, :], y_ps[Q * r:Q * r + Q, g, :], ACT.Copy)
                n.then_inc(y_out_act, 1)

            def take_z(s):
                if not exists(s):
                    return
                act.wait_ge(z_ready, done(s))
                act.wait_ge(par_made, done(s))
                at_least(act, z_stored[buf(s)], DMA * uses(s))
                nc.scalar.activation(z_out[buf(s)][:, :].rearrange("c (n q) -> c q n", q=PH), z_ps[:, :, :],
                                     ACT.Identity, bias=par[buf(s)][:, NK + 1:NK + 2]).then_inc(z_read, 1)

            for k in range(4):
                split_phases((0, k))
            put_taps(act, (2, 3), lambda o, i: nc.scalar.activation(o, i, ACT.Copy), taps_placed_act)
            split_phases((1, 0))
            act.wait_ge(weights_loaded, DMA * 11)
            act.wait_ge(mlp_mm, 1)
            nc.scalar.activation(h1[:, :], ps[:, 6, 0:NS], ACT.Gelu, bias=cols[:, 1:2]).then_inc(mlp_act, 1)
            act.wait_ge(mlp_mm, 2)
            nc.scalar.activation(h2[:, :], ps[:, 7, 0:NS], ACT.Gelu, bias=cols[:, 2:3]).then_inc(mlp_act, 1)
            act.wait_ge(soft, 3)
            nc.scalar.activation(expd[:, :], logit[:, :], ACT.Exp, bias=ntop[:, 0:1]).then_inc(mlp_act, 1)

            def slot(s):
                take_z(after(s, -2))
                take_y(s, 0)
                split_phases(after(s, AHEAD - 2))
                for g in range(1, G):
                    take_y(s, g)

            pipeline(act, slot)

        @block.vector
        def _(dve):
            def split_x(s):
                if not exists(s):
                    return
                dve.wait_ge(x_moved[pair_buf(s)], DMA * PH * G * (s[0] + 1))
                at_least(dve, y_ready, done(s, G, lag=-2))
                nc.vector.tensor_copy(x_hi[buf(s)][:, :, 1:N + 1], x_cv[pair_buf(s)][:, :, buf(s), :]).then_inc(x_hi_made, 1)
                dve.wait_ge(x_hi_made, done(s))
                nc.vector.tensor_tensor(x_lo[buf(s)][:, :, 1:N + 1], x_cv[pair_buf(s)][:, :, buf(s), :],
                                        x_hi[buf(s)][:, :, 1:N + 1].bitcast(F32), ALU.subtract).then_inc(x_lo_made, 1)

            def take_y(s):
                if not exists(s):
                    return
                dve.wait_ge(y_ready, done(s, G))
                g = G - 1
                for r in range(ACT_PHASES, PH):
                    n = nc.vector.tensor_copy(y_in[buf(s)][Q * g:Q * g + Q, r, :], y_ps[Q * r:Q * r + Q, g, :])
                n.then_inc(y_out_dve, 1)

            def split_y(s):
                if not exists(s):
                    return
                dve.wait_ge(y_out_act, done(s, G))
                dve.wait_ge(y_out_dve, done(s))
                dve.wait_ge(y_moved[buf(s)], DMA * PH * (uses(s) + 1))
                dve.wait_ge(par_made, done(s))
                at_least(dve, z_ready, done(s, lag=-1))
                y_bias = par[buf(s)][:, NK:NK + 1]
                nc.vector.tensor_scalar(y_hi[:, :, :], y_in[buf(s)][:, :, :], y_bias, None,
                                        ALU.add).then_inc(y_hi_made, 1)
                dve.wait_ge(y_hi_made, done(s))
                nc.vector.scalar_tensor_tensor(out=y_lo[:, :, :], in0=y_in[buf(s)][:, :, :], scalar=y_bias,
                                               in1=y_hi[:, :, :].bitcast(F32), op0=ALU.add,
                                               op1=ALU.subtract).then_inc(y_lo_made, 1)

            dve.wait_ge(conv_w_loaded, DMA)
            nc.vector.tensor_copy(cw_rep[:, :, :, :],
                                  cw_nat[:, :, :].rearrange("o c k -> o k c").unsqueeze(2)
                                  .broadcast_to([P, K, PH, CG])).then_inc(taps_spread, 1)
            put_taps(dve, (0, 1), nc.vector.tensor_copy, taps_placed_dve)
            dve.wait_ge(taps_placed_act, 1)
            dve.wait_ge(taps_placed_dve, 1)
            dve.wait_ge(ident_made, 2)
            for g in range(G):
                nc.vector.tensor_tensor(cw_f[:, g, 1, :], cw_f[:, g, 1, :], ident[:, :],
                                        ALU.add).then_inc(taps_placed_dve, 1)
            dve.wait_ge(taps_placed_dve, 1 + G)
            nc.vector.tensor_copy(cw_hi[:, :, :, :], cw_f[:, :, :, :]).then_inc(conv_w_ready, 1)
            dve.wait_ge(conv_w_ready, 1)
            nc.vector.tensor_tensor(cw_lo[:, :, :, :], cw_f[:, :, :, :], cw_hi[:, :, :, :].bitcast(F32),
                                    ALU.subtract).then_inc(conv_w_ready, 1)
            dve.wait_ge(cond_turned, 1)
            nc.vector.tensor_copy(cond_t[:, :], ps[:, 3, 0:NS]).then_inc(cond_copied, 1)
            nc.vector.tensor_copy(ctxw_t[:, :], ps[:, 3, P:2 * P]).then_inc(cond_copied, 1)
            split_x((0, 0))
            dve.wait_ge(ctx_mm, 1)
            nc.vector.tensor_scalar(table[:, :, NK:NK + 1].rearrange("p s a -> p (s a)"), ps[:, 3, 0:NS],
                                    cols[:, 0:1], None, ALU.add).then_inc(table_made, 1)
            dve.wait_ge(mixw_turned, 1)
            nc.vector.tensor_copy(mixw_t[:, :, :].rearrange("i k o -> i (k o)"),
                                  ps[:, 4:6, :].rearrange("i b n -> i (b n)")).then_inc(mixw_copied, 1)
            dve.wait_ge(mlp_mm, 3)
            nc.vector.tensor_copy(logit[:, :], ps[0:NS, 6, 0:NK]).then_inc(soft, 1)
            dve.wait_ge(soft, 1)
            nc.vector.tensor_reduce(top[:, :], logit[:, :], AX.X, ALU.max).then_inc(soft, 1)
            dve.wait_ge(soft, 2)
            nc.vector.tensor_scalar(ntop[:, :], top[:, :], -1.0, None, ALU.mult).then_inc(soft, 1)
            dve.wait_ge(mlp_act, 3)
            nc.vector.tensor_reduce(total[:, :], expd[:, :], AX.X, ALU.add).then_inc(soft, 1)
            dve.wait_ge(soft, 4)
            nc.vector.reciprocal(inv[:, :], total[:, :]).then_inc(soft, 1)
            dve.wait_ge(soft, 5)
            nc.vector.tensor_scalar(att[:, :], expd[:, :], inv[:, 0:1], None, ALU.mult).then_inc(soft, 1)
            dve.wait_ge(soft, 6)
            nc.vector.tensor_tensor(att_diag[:, :, :], ident[0:NS, 0:NS].unsqueeze(2).broadcast_to([NS, NS, NK]),
                                    att[:, :].unsqueeze(1).broadcast_to([NS, NS, NK]), ALU.mult).then_inc(soft, 1)
            dve.wait_ge(att_mm, 1)
            nc.vector.tensor_copy(att_t[:, :], ps[0:NK, 7, 0:NS]).then_inc(soft, 1)
            dve.wait_ge(aggb_mm, 1)
            nc.vector.tensor_copy(table[:, :, NK + 1:NK + 2].rearrange("p s a -> p (s a)"),
                                  ps[:, 6, 0:NS]).then_inc(table_made, 1)
            dve.wait_ge(att_mm, 2)
            nc.vector.tensor_copy(table[:, :, 0:NK], ps[:, 7, :].rearrange("p (s k) -> p s k", k=NK)
                                  ).then_inc(table_made, 1)

            def slot(s):
                split_x(after(s, 1))
                split_y(after(s, -1))
                take_y(s)

            pipeline(dve, slot)

        @block.gpsimd
        def _(pool):
            nc.gpsimd.memset(ident[:, :], 0.0).then_inc(ident_made, 1)
            pool.wait_ge(ident_made, 1)
            nc.gpsimd.affine_select(out=ident[:, :], in_=ident[:, :], compare_op=ALU.not_equal, fill=1.0,
                                    base=0, pattern=[[-1, P]], channel_multiplier=1).then_inc(ident_made, 1)
            nc.gpsimd.memset(cw_f[:, :, :, :], 0.0).then_inc(cw_cleared, 1)
            for part in (x_hi, x_lo):
                for k in range(2):
                    nc.gpsimd.memset(part[k][:, :, 0:N + 2:N + 1].bitcast(F32), 0.0).then_inc(halos_cleared, 1)
            nc.gpsimd.memset(ones[:, :], 1.0).then_inc(consts_made, 1)

            def mix_matrix(s):
                if not exists(s):
                    return
                at_least(pool, z_read, done(s, lag=-2))
                pool.wait_ge(table_made, 3)
                nc.gpsimd.tensor_copy(par[buf(s)][:, :], table[:, number(s), :]).then_inc(par_made, 1)
                pool.wait_ge(par_made, done(s))
                nc.gpsimd.tensor_tensor(mix_prod[:, :, :], mixw_t[:, :, :],
                                        par[buf(s)][:, 0:NK].unsqueeze(2).broadcast_to([P, NK, P]),
                                        ALU.mult).then_inc(prod_made, 1)
                pool.wait_ge(prod_made, done(s))
                for n, half in enumerate((4, 2)):
                    nc.gpsimd.tensor_tensor(mix_prod[:, 0:half, :], mix_prod[:, 0:half, :],
                                            mix_prod[:, half:2 * half, :], ALU.add).then_inc(mix_sum, 1)
                    pool.wait_ge(mix_sum, done(s, 3, lag=-1) + n + 1)
                nc.gpsimd.tensor_tensor(mix_sum_f[:, :], mix_prod[:, 0, :], mix_prod[:, 1, :],
                                        ALU.add).then_inc(mix_sum, 1)
                pool.wait_ge(mix_sum, done(s, 3))
                nc.gpsimd.tensor_tensor(mix_f[:, :], mix_sum_f[:, :], ident[:, :], ALU.add)
                nc.gpsimd.tensor_tensor(mix_hi[buf(s)][:, :], mix_sum_f[:, :], ident[:, :],
                                        ALU.add).then_inc(mix_hi_made, 1)
                pool.wait_ge(mix_hi_made, done(s))
                nc.gpsimd.tensor_tensor(mix_lo[buf(s)][:, :], mix_f[:, :], mix_hi[buf(s)][:, :].bitcast(F32),
                                        ALU.subtract).then_inc(mix_made, 1)
                pool.wait_ge(mix_made, done(s))

            pool.wait_ge(table_made, 3)
            pool.wait_ge(mixw_copied, 1)
            pipeline(pool, mix_matrix)


_INS = ["x", "cond_128", "fside_S_0", "L0_cond_weight", "L0_cond_c_weight", "L1_cond_W0", "L1_cond_b0",
        "L1_cond_W1", "L1_cond_b1", "L1_cond_W2", "L1_cond_b2", "L1_cond_weight", "L1_cond_bias_k"]


def kernel(**inputs):
    import numpy as np
    import concourse.bacc as bacc
    from concourse.bass_utils import run_bass_kernel_spmd

    nc = bacc.Bacc("TRN2", target_bir_lowering=False, num_devices=1)
    arrays, args = {}, []
    for name in _INS:
        a = np.ascontiguousarray(inputs[name])
        arrays[f"in_{name}_dram"] = a
        args.append(nc.dram_tensor(f"in_{name}_dram", a.shape, mybir.dt.from_np(a.dtype), kind="ExternalInput").ap())
    shape = inputs["x"].shape
    args.append(nc.dram_tensor("out_dram", shape, F32, kind="ExternalOutput").ap())
    cond_resid_kernel(nc, *args)
    r = run_bass_kernel_spmd(nc, [arrays], core_ids=[0])
    return r.results[0]["out_dram"]
```

```python
from contextlib import ExitStack

import concourse.bass as bass
from concourse import mybir

F32 = mybir.dt.float32
F32R = mybir.dt.float32r
ALU = mybir.AluOpType
ACT = mybir.ActivationFunctionType
AX = mybir.AxisListType

P = 128
PH = 4
U = 4
Q = 32
DMA = 16
AHEAD = 7
ACT_PHASES = 1


def after(sample, lag):
    n, k = sample
    return n + (k + lag) // U, (k + lag) % U


def number(sample):
    n, k = sample
    return n * U + k


def done(sample, each=1, lag=0):
    n, k = sample
    return n * (U * each) + (k + 1 + lag) * each


def buf(sample):
    return sample[1] % 2


def uses(sample):
    n, k = sample
    return n * (U // 2) + k // 2


def pair_buf(sample):
    return sample[1] // 2


def at_least(eng, sem, value):
    if isinstance(value, int) and value <= 0:
        return
    eng.wait_ge(sem, value)


def cond_resid_kernel(nc, x, cond, bias, conv_w, ctx_w, w0, b0, w1, b1, w2, b2, mix_w, mix_b, out):
    NS, C, T = x.shape
    CG, K = conv_w.shape[1:]
    G = C // CG
    NK = mix_b.shape[0]
    N = T // PH
    PAD = K // 2
    ROUNDS = NS // U
    PC = NK + 2
    assert C == P and CG == Q and G == PH and N == 512 and K <= 2 * PH + 1 and NS % U == 0

    with ExitStack() as stack:
        def sb(name, shape, dt=F32):
            return stack.enter_context(nc.sbuf_tensor(name, shape, dt))

        def sem(name):
            return stack.enter_context(nc.semaphore(name))

        def two(make, name, *args):
            return [make(f"{name}{k}", *args) for k in range(2)]

        x_in = two(sb, "x_in", [P, T])
        x_ph = two(sb, "x_ph", [P, PH, 2, N])
        x_cv = two(sb, "x_cv", [P, G, 2, N])
        x_hi = two(sb, "x_hi", [P, G, N + 2], F32R)
        x_lo = two(sb, "x_lo", [P, G, N + 2], F32R)
        y_st = two(sb, "y_st", [P, N])
        y_in = two(sb, "y_in", [P, PH, N])
        y_hi = sb("y_hi", [P, PH, N], F32R)
        y_lo = sb("y_lo", [P, PH, N], F32R)
        z_out = two(sb, "z_out", [P, T])
        par = two(sb, "par", [P, PC])
        mix_prod = sb("mix_prod", [P, NK, P])
        mix_sum_f = sb("mix_sum_f", [P, P])
        mix_f = sb("mix_f", [P, P])
        mix_hi = two(sb, "mix_hi", [P, P], F32R)
        mix_lo = two(sb, "mix_lo", [P, P], F32R)

        cw_hi = sb("cw_hi", [P, G, 3, P], F32R)
        cw_lo = sb("cw_lo", [P, G, 3, P], F32R)
        cw_f = z_out[0][:, 0:G * 3 * P].rearrange("p (g b o) -> p g b o", g=G, b=3)
        cw_rep = z_out[1][:, 0:K * P].rearrange("o (k q c) -> o k q c", k=K, q=PH)
        cw_nat = z_out[1][:, K * P:K * P + CG * K].rearrange("o (c k) -> o c k", k=K)
        ctxw_nat = sb("ctxw_nat", [P, P])
        cond_nat = sb("cond_nat", [NS, P])
        cond_t = sb("cond_t", [P, NS])
        ctxw_t = sb("ctxw_t", [P, P])
        w0_sb = sb("w0_sb", [P, P])
        w1_sb = sb("w1_sb", [P, P])
        w2_sb = sb("w2_sb", [P, NK])
        b2_sb = sb("b2_sb", [1, NK])
        cols = sb("cols", [P, 3])
        mixb_sb = sb("mixb_sb", [NK, P])
        mixw_nat = y_in[0][:, 0:2, :].rearrange("o q n -> o (q n)").rearrange("o (k i) -> o k i", k=NK)
        mixw_t = sb("mixw_t", [P, NK, P])
        h1 = sb("h1", [P, NS])
        h2 = sb("h2", [P, NS])
        ident = sb("ident", [P, P])
        ones = sb("ones", [NS, P])
        logit = sb("logit", [NS, NK])
        top = sb("top", [NS, 1])
        ntop = sb("ntop", [NS, 1])
        expd = sb("expd", [NS, NK])
        total = sb("total", [NS, 1])
        inv = sb("inv", [NS, 1])
        att = sb("att", [NS, NK])
        mixb_t = sb("mixb_t", [P, NK])
        aggb_prod = mix_prod[:, :, :].rearrange("p k o -> p (k o)")[:, 0:NS * NK].rearrange("p (s k) -> p s k", k=NK)
        att_diag = sb("att_diag", [NS, NS, NK])
        table = sb("table", [P, NS, PC])

        ps = stack.enter_context(nc.psum_tensor("ps", [P, 8, 512], F32))
        y_ps = ps[:, 0:G, :]
        z_ps = ps[:, G:G + PH, :]
        halves = [(slice(0, N // 2), z_ps), (slice(N // 2, N), y_ps)]

        weights_loaded = sem("weights_loaded")
        conv_w_loaded = sem("conv_w_loaded")
        ident_made = sem("ident_made")
        consts_made = sem("consts_made")
        cw_cleared = sem("cw_cleared")
        halos_cleared = sem("halos_cleared")
        taps_spread = sem("taps_spread")
        taps_turned = sem("taps_turned")
        taps_placed_act = sem("taps_placed_act")
        taps_placed_dve = sem("taps_placed_dve")
        conv_w_ready = sem("conv_w_ready")
        cond_turned = sem("cond_turned")
        cond_copied = sem("cond_copied")
        mixw_turned = sem("mixw_turned")
        mixw_copied = sem("mixw_copied")
        mlp_mm = sem("mlp_mm")
        mlp_act = sem("mlp_act")
        soft = sem("soft")
        ctx_mm = sem("ctx_mm")
        att_mm = sem("att_mm")
        table_made = sem("table_made")

        x0_by_dve = sem("x0_by_dve")
        x0_by_pool = sem("x0_by_pool")
        x1_by_pool = sem("x1_by_pool")
        x_loaded = two(sem, "x_loaded")
        x_split_ph = sem("x_split_ph")
        x_moved = two(sem, "x_moved")
        x_hi_made = sem("x_hi_made")
        x_lo_made = sem("x_lo_made")
        y_ready = sem("y_ready")
        y_out_act = sem("y_out_act")
        y_out_dve = sem("y_out_dve")
        y_moved = two(sem, "y_moved")
        y_hi_made = sem("y_hi_made")
        y_lo_made = sem("y_lo_made")
        par_made = sem("par_made")
        prod_made = sem("prod_made")
        mix_sum = sem("mix_sum")
        mix_hi_made = sem("mix_hi_made")
        mix_made = sem("mix_made")
        z_ready = sem("z_ready")
        z_read = sem("z_read")
        z_stored = two(sem, "z_stored")

        def exists(sample):
            n, _ = sample
            return not isinstance(n, int) or 0 <= n < ROUNDS

        def is_sample(s, b):
            return isinstance(s[0], int) and number(s) == b

        def pipeline(eng, slot):
            last = ROUNDS - (AHEAD + U - 1) // U
            for k in range(U):
                slot((0, k))
            with eng.Fori(1, last) as n:
                for k in range(U):
                    slot((n, k))
            for s in range(U * last, NS + 2):
                slot((s // U, s % U))

        block = stack.enter_context(nc.Block())

        @block.sync
        def _(sp):
            def ahead(*values):
                for v in values:
                    if not isinstance(v, int):
                        sp.compute_val(v)
                return values

            def load(s):
                if not exists(s):
                    return
                b, split = ahead(number(s), done(s, lag=-2))
                at_least(sp, x_split_ph, split)
                sp.dma_start(x_in[buf(s)][:, :], x[b, :, :]).then_inc(x_loaded[buf(s)], DMA)

            def move_x(s, phases, first=0, groups=range(G)):
                if not exists(s):
                    return
                b = pair_buf(s)
                split, low = ahead(done(s, lag=1), done(s, lag=-3))
                sp.wait_ge(x_split_ph, split)
                at_least(sp, x_lo_made, low)
                for d in (2, 3, 0, 1):
                    for n, p in enumerate(phases):
                        g = (d + 2 * n) % G
                        if g in groups:
                            sp.dma_start(x_cv[b][Q * p:Q * p + Q, g, first:2, :],
                                         x_ph[b][Q * g:Q * g + Q, p, first:2, :]).then_inc(x_moved[b], DMA)

            def move_y(s):
                if not exists(s):
                    return
                taken, low = ahead(done(s, G, lag=-1) + 1, done(s, lag=-2))
                sp.wait_ge(y_out_act, taken)
                at_least(sp, y_lo_made, low)
                for r in (0, 2, 1, 3):
                    sp.dma_start(y_in[buf(s)][0:Q, r, :],
                                 y_st[buf(s)][Q * r:Q * r + Q, :]).then_inc(y_moved[buf(s)], DMA)

            def store(s):
                if not exists(s):
                    return
                if is_sample(s, NS - 1):
                    for h, (cols_h, _) in enumerate(halves):
                        sp.wait_ge(z_read, done(s, lag=-1) + h + 1)
                        t = slice(PH * cols_h.start, PH * cols_h.stop)
                        sp.dma_start(out[number(s), :, t], z_out[buf(s)][:, t]).then_inc(z_stored[buf(s)], DMA)
                    return
                b, read = ahead(number(s), done(s))
                sp.wait_ge(z_read, read)
                sp.dma_start(out[b, :, :], z_out[buf(s)][:, :]).then_inc(z_stored[buf(s)], DMA)

            sp.dma_start(cw_nat[:, :, :], conv_w[:, :, :]).then_inc(conv_w_loaded, DMA)
            load((0, 0))
            load((0, 1))
            for to, of in (
                (cond_nat[:, :], cond[:, :]),
                (ctxw_nat[:, :], ctx_w[:, :]),
                (w0_sb[:, :], w0[:, :]),
                (w1_sb[:, :], w1[:, :]),
                (w2_sb[:, :], w2[:, :]),
                (b2_sb[:, :], b2.rearrange("(a k) -> a k", a=1)),
                (cols[:, 0:1], bias.rearrange("(c a) -> c a", a=1)),
                (cols[:, 1:2], b0.rearrange("(c a) -> c a", a=1)),
                (cols[:, 2:3], b1.rearrange("(c a) -> c a", a=1)),
                (mixb_sb[:, :], mix_b[:, :]),
                (mixw_nat[:, :, :], mix_w.rearrange("k o i a -> o k (i a)")),
            ):
                sp.dma_start(to, of).then_inc(weights_loaded, DMA)
            sp.wait_ge(x0_by_dve, 1)
            sp.wait_ge(x0_by_pool, PH)
            load((0, 2))
            load((0, 3))
            move_x((0, 0), (0, 2, 1, 3), first=1, groups=range(G - 2))
            load((1, 0))
            load((1, 1))
            move_x((0, 2), (0, 2))
            move_y((0, 0))
            move_x((0, 2), (1, 3))
            load((1, 2))

            def slot(s):
                store(after(s, -2))
                if not is_sample(s, 0):
                    move_y(s)
                    if s[1] % 2:
                        move_x(after(s, 3), (0, 2))
                    else:
                        move_x(after(s, 2), (1, 3))
                load(after(s, AHEAD))

            pipeline(sp, slot)
            sp.wait_ge(z_stored[0], DMA * (NS // 2))
            sp.wait_ge(z_stored[1], DMA * (NS // 2 + 1))

        @block.tensor
        def _(pe):
            pe.wait_ge(ident_made, 2)
            pe.wait_ge(taps_spread, 1)
            for k in range(K):
                mm = pe.transpose(ps[:, k // 4, k % 4 * P:k % 4 * P + P],
                                  cw_rep[:, k, :, :].rearrange("o q c -> o (q c)"), ident[:, :])
            mm.then_inc(taps_turned, 1)
            pe.wait_ge(weights_loaded, DMA * 11)
            pe.transpose(ps[:, 3, 0:NS], cond_nat[:, :], ident[0:NS, 0:NS])
            pe.transpose(ps[:, 3, 3 * P:3 * P + NK], mixb_sb[:, :], ident[0:NK, 0:NK])
            pe.transpose(ps[:, 3, P:2 * P], ctxw_nat[:, :], ident[:, :]).then_inc(cond_turned, 1)
            for k in range(NK):
                mm = pe.transpose(ps[:, 4 + k // 4, k % 4 * P:k % 4 * P + P], mixw_nat[:, k, :], ident[:, :])
            mm.then_inc(mixw_turned, 1)
            pe.wait_ge(cond_copied, 3)
            pe.matmul(ps[:, 6, 0:NS], w0_sb[:, :], cond_t[:, :], start=True, stop=True).then_inc(mlp_mm, 1)
            pe.matmul(ps[:, 3, 0:NS], ctxw_t[:, :], cond_t[:, :], start=True, stop=True).then_inc(ctx_mm, 1)
            pe.wait_ge(mlp_act, 1)
            pe.matmul(ps[:, 7, 0:NS], w1_sb[:, :], h1[:, :], start=True, stop=True).then_inc(mlp_mm, 1)
            pe.wait_ge(mlp_act, 2)
            pe.wait_ge(consts_made, 1)
            pe.matmul(ps[0:NS, 6, 0:NK], h2[:, :], w2_sb[:, :], start=True, stop=False)
            pe.matmul(ps[0:NS, 6, 0:NK], ones[0:1, 0:NS], b2_sb[:, :], start=False, stop=True).then_inc(mlp_mm, 1)

            def attention():
                pe.wait_ge(soft, 7)
                pe.matmul(ps[:, 7, :], ones[:, :], att_diag[:, :, :].rearrange("p s k -> p (s k)"),
                          start=True, stop=True).then_inc(att_mm, 1)

            def conv(s):
                if not exists(s):
                    return
                pe.wait_ge(x_lo_made, done(s))
                for g in range(G):
                    at_least(pe, y_out_act, done(s, G, lag=-2) + g + 1)
                    if g == G - 1:
                        at_least(pe, y_out_dve, done(s, lag=-1))
                    terms = [(w, xx, b) for w, xx in ((cw_hi, x_hi), (cw_lo, x_hi), (cw_hi, x_lo)) for b in range(3)]
                    for n, (w, xx, b) in enumerate(terms):
                        mm = pe.matmul(y_ps[:, g, :], w[:, g, b, :], xx[buf(s)][:, g, b:b + N],
                                       start=n == 0, stop=n == len(terms) - 1)
                    mm.then_inc(y_ready, 1)
                    if is_sample(s, 0) and g == 2:
                        attention()

            def mix(s):
                if not exists(s):
                    return
                if is_sample(s, NS - 1):
                    mix_last(s)
                    return
                pe.wait_ge(y_lo_made, done(s))
                pe.wait_ge(mix_made, done(s))
                at_least(pe, z_read, done(s, lag=-1))
                for r in range(PH):
                    terms = [(mix_hi, y_hi), (mix_lo, y_hi), (mix_hi, y_lo)]
                    for n, (w, yy) in enumerate(terms):
                        mm = pe.matmul(z_ps[:, r, :], w[buf(s)][:, :], yy[:, r, :],
                                       start=n == 0, stop=n == len(terms) - 1)
                mm.then_inc(z_ready, 1)

            def mix_last(s):
                pe.wait_ge(mix_made, done(s))
                for h, (cols_h, banks) in enumerate(halves):
                    pe.wait_ge(y_lo_made, done(s, lag=-1) + h + 1)
                    if h == 0:
                        pe.wait_ge(z_read, done(s, lag=-1))
                    else:
                        pe.wait_ge(y_out_act, done(s, G))
                        pe.wait_ge(y_out_dve, done(s))
                    for r in range(PH):
                        terms = [(mix_hi, y_hi), (mix_lo, y_hi), (mix_hi, y_lo)]
                        for n, (w, yy) in enumerate(terms):
                            mm = pe.matmul(banks[:, r, 0:N // 2], w[buf(s)][:, :], yy[:, r, cols_h],
                                           start=n == 0, stop=n == len(terms) - 1)
                    mm.then_inc(z_ready, 1)

            def slot(s):
                conv(s)
                mix(after(s, -1))

            pe.wait_ge(conv_w_ready, 2)
            pe.wait_ge(halos_cleared, 4)
            pe.wait_ge(table_made, 1)
            pipeline(pe, slot)

        def place(k, q):
            r = (q - k) % PH
            return r, (k - PAD + r - q) // PH + 1

        def put_taps(eng, phases, write, placed):
            eng.wait_ge(taps_turned, 1)
            eng.wait_ge(cw_cleared, 1)
            for q in phases:
                for k in range(K):
                    r, b = place(k, q)
                    n = write(cw_f[Q * q:Q * q + Q, :, b, Q * r:Q * r + Q],
                              ps[Q * q:Q * q + Q, k // 4, k % 4 * P:k % 4 * P + P].rearrange("c (g o) -> c g o", g=G))
            n.then_inc(placed, 1)

        def move_x0(eng, groups, copy, moved):
            eng.wait_ge(x_loaded[0], DMA)
            for g in groups:
                for p in range(PH):
                    n = copy(x_cv[0][Q * p:Q * p + Q, g, 0, :],
                             x_in[0][Q * g:Q * g + Q, :].rearrange("c (n q) -> c q n", q=PH)[:, p, :])
            n.then_inc(moved, 1)

        @block.scalar
        def _(act):
            def split_phases(s):
                if not exists(s):
                    return
                act.wait_ge(x_loaded[buf(s)], DMA * (uses(s) + 1))
                at_least(act, x_moved[pair_buf(s)], DMA * PH * G * s[0])
                nc.scalar.activation(x_ph[pair_buf(s)][:, :, buf(s), :], x_in[buf(s)][:, :].rearrange("c (n q) -> c q n", q=PH),
                                     ACT.Copy).then_inc(x_split_ph, 1)

            def take_y(s, g):
                if not exists(s):
                    return
                act.wait_ge(y_ready, done(s, G, lag=-1) + g + 1)
                if g == 0:
                    at_least(act, y_moved[buf(s)], DMA * PH * uses(s))
                    nc.scalar.activation(y_st[buf(s)][:, :], y_ps[:, 0, :], ACT.Copy).then_inc(y_out_act, 1)
                    return
                if g == 1:
                    at_least(act, y_lo_made, done(s, lag=-2))
                for r in range(ACT_PHASES if g == G - 1 else PH):
                    n = nc.scalar.activation(y_in[buf(s)][Q * g:Q * g + Q, r, :], y_ps[Q * r:Q * r + Q, g, :], ACT.Copy)
                n.then_inc(y_out_act, 1)

            def take_z(s):
                if not exists(s):
                    return
                if is_sample(s, NS - 1):
                    act.wait_ge(par_made, done(s))
                    act.wait_ge(z_stored[buf(s)], DMA * uses(s))
                    for h, (cols_h, banks) in enumerate(halves):
                        act.wait_ge(z_ready, done(s, lag=-1) + h + 1)
                        nc.scalar.activation(
                            z_out[buf(s)][:, :].rearrange("c (n q) -> c q n", q=PH)[:, :, cols_h],
                            banks[:, :, 0:N // 2], ACT.Identity,
                            bias=par[buf(s)][:, NK + 1:NK + 2]).then_inc(z_read, 1)
                    return
                act.wait_ge(z_ready, done(s))
                act.wait_ge(par_made, done(s))
                at_least(act, z_stored[buf(s)], DMA * uses(s))
                nc.scalar.activation(z_out[buf(s)][:, :].rearrange("c (n q) -> c q n", q=PH), z_ps[:, :, :],
                                     ACT.Identity, bias=par[buf(s)][:, NK + 1:NK + 2]).then_inc(z_read, 1)

            def copy(o, i):
                return nc.scalar.activation(o, i, ACT.Copy)

            move_x0(act, (0, 1), copy, x_split_ph)
            put_taps(act, (2, 3), copy, taps_placed_act)
            split_phases((0, 1))
            act.wait_ge(weights_loaded, DMA * 11)
            act.wait_ge(mlp_mm, 1)
            nc.scalar.activation(h1[:, :], ps[:, 6, 0:NS], ACT.Gelu, bias=cols[:, 1:2]).then_inc(mlp_act, 1)
            act.wait_ge(x_split_ph, 2)
            g = G - 2
            for p in range(PH):
                n = copy(x_cv[0][Q * p:Q * p + Q, g, 1, :], x_ph[0][Q * g:Q * g + Q, p, 1, :])
            n.then_inc(x_moved[0], DMA * PH)
            act.wait_ge(mlp_mm, 2)
            nc.scalar.activation(h2[:, :], ps[:, 7, 0:NS], ACT.Gelu, bias=cols[:, 2:3]).then_inc(mlp_act, 1)
            split_phases((0, 2))
            split_phases((0, 3))
            act.wait_ge(soft, 3)
            nc.scalar.activation(expd[:, :], logit[:, :], ACT.Exp, bias=ntop[:, 0:1]).then_inc(mlp_act, 1)

            def slot(s):
                take_z(after(s, -2))
                take_y(s, 0)
                if is_sample(s, 1):
                    split_phases((1, 1))
                elif not is_sample(s, 0):
                    split_phases(after(s, AHEAD - 2))
                for g in range(1, G):
                    take_y(s, g)
                if is_sample(s, 0):
                    split_phases((1, 0))
                elif is_sample(s, 1):
                    split_phases((1, 2))

            pipeline(act, slot)

        @block.vector
        def _(dve):
            def split_x(s):
                if not exists(s):
                    return
                if is_sample(s, 0):
                    dve.wait_ge(x_split_ph, 1)
                    dve.wait_ge(x0_by_dve, 1)
                    dve.wait_ge(x0_by_pool, PH)
                else:
                    dve.wait_ge(x_moved[pair_buf(s)], DMA * PH * G * (s[0] + 1))
                at_least(dve, y_ready, done(s, G, lag=-2))
                nc.vector.tensor_copy(x_hi[buf(s)][:, :, 1:N + 1], x_cv[pair_buf(s)][:, :, buf(s), :]).then_inc(x_hi_made, 1)
                dve.wait_ge(x_hi_made, done(s))
                nc.vector.tensor_tensor(x_lo[buf(s)][:, :, 1:N + 1], x_cv[pair_buf(s)][:, :, buf(s), :],
                                        x_hi[buf(s)][:, :, 1:N + 1].bitcast(F32), ALU.subtract).then_inc(x_lo_made, 1)

            def take_y(s):
                if not exists(s):
                    return
                dve.wait_ge(y_ready, done(s, G))
                g = G - 1
                for r in range(ACT_PHASES, PH):
                    n = nc.vector.tensor_copy(y_in[buf(s)][Q * g:Q * g + Q, r, :], y_ps[Q * r:Q * r + Q, g, :])
                n.then_inc(y_out_dve, 1)

            def split_y(s):
                if not exists(s):
                    return
                dve.wait_ge(y_out_act, done(s, G))
                dve.wait_ge(y_out_dve, done(s))
                dve.wait_ge(y_moved[buf(s)], DMA * PH * (uses(s) + 1))
                dve.wait_ge(par_made, done(s))
                at_least(dve, z_ready, done(s, lag=-1))
                y_bias = par[buf(s)][:, NK:NK + 1]
                for h, (c, _) in enumerate(halves if is_sample(s, NS - 1) else [(slice(0, N), None)]):
                    nc.vector.tensor_scalar(y_hi[:, :, c], y_in[buf(s)][:, :, c], y_bias, None,
                                            ALU.add).then_inc(y_hi_made, 1)
                    dve.wait_ge(y_hi_made, done(s) + h)
                    nc.vector.scalar_tensor_tensor(out=y_lo[:, :, c], in0=y_in[buf(s)][:, :, c], scalar=y_bias,
                                                   in1=y_hi[:, :, c].bitcast(F32), op0=ALU.add,
                                                   op1=ALU.subtract).then_inc(y_lo_made, 1)

            dve.wait_ge(conv_w_loaded, DMA)
            nc.vector.tensor_copy(cw_rep[:, :, :, :],
                                  cw_nat[:, :, :].rearrange("o c k -> o k c").unsqueeze(2)
                                  .broadcast_to([P, K, PH, CG])).then_inc(taps_spread, 1)
            move_x0(dve, (2,), nc.vector.tensor_copy, x0_by_dve)
            put_taps(dve, (0, 1), nc.vector.tensor_copy, taps_placed_dve)
            dve.wait_ge(cond_turned, 1)
            nc.vector.tensor_copy(cond_t[:, :], ps[:, 3, 0:NS]).then_inc(cond_copied, 1)
            nc.vector.tensor_copy(ctxw_t[:, :], ps[:, 3, P:2 * P]).then_inc(cond_copied, 1)
            nc.vector.tensor_copy(mixb_t[:, :], ps[:, 3, 3 * P:3 * P + NK]).then_inc(cond_copied, 1)
            dve.wait_ge(taps_placed_act, 1)
            dve.wait_ge(taps_placed_dve, 1)
            dve.wait_ge(ident_made, 2)
            nc.vector.tensor_tensor(cw_f[:, :, 1, :], cw_f[:, :, 1, :],
                                    ident[:, :].unsqueeze(1).broadcast_to([P, G, P]),
                                    ALU.add).then_inc(taps_placed_dve, 1)
            dve.wait_ge(taps_placed_dve, 2)
            nc.vector.tensor_copy(cw_hi[:, :, :, :], cw_f[:, :, :, :]).then_inc(conv_w_ready, 1)
            dve.wait_ge(conv_w_ready, 1)
            nc.vector.tensor_tensor(cw_lo[:, :, :, :], cw_f[:, :, :, :], cw_hi[:, :, :, :].bitcast(F32),
                                    ALU.subtract).then_inc(conv_w_ready, 1)
            dve.wait_ge(ctx_mm, 1)
            nc.vector.tensor_scalar(table[:, :, NK:NK + 1].rearrange("p s a -> p (s a)"), ps[:, 3, 0:NS],
                                    cols[:, 0:1], None, ALU.add).then_inc(table_made, 1)
            split_x((0, 0))
            dve.wait_ge(mlp_mm, 3)
            nc.vector.tensor_copy(logit[:, :], ps[0:NS, 6, 0:NK]).then_inc(soft, 1)
            dve.wait_ge(soft, 1)
            nc.vector.tensor_reduce(top[:, :], logit[:, :], AX.X, ALU.max).then_inc(soft, 1)
            dve.wait_ge(soft, 2)
            nc.vector.tensor_scalar(ntop[:, :], top[:, :], -1.0, None, ALU.mult).then_inc(soft, 1)
            dve.wait_ge(mixw_turned, 1)
            nc.vector.tensor_copy(mixw_t[:, :, :].rearrange("i k o -> i (k o)"),
                                  ps[:, 4:6, :].rearrange("i b n -> i (b n)")).then_inc(mixw_copied, 1)
            split_x((0, 1))
            dve.wait_ge(mlp_act, 3)
            nc.vector.tensor_reduce(total[:, :], expd[:, :], AX.X, ALU.add).then_inc(soft, 1)
            dve.wait_ge(soft, 4)
            nc.vector.reciprocal(inv[:, :], total[:, :]).then_inc(soft, 1)
            dve.wait_ge(soft, 5)
            nc.vector.tensor_scalar(att[:, :], expd[:, :], inv[:, 0:1], None, ALU.mult).then_inc(soft, 1)
            dve.wait_ge(soft, 6)
            nc.vector.tensor_tensor(att_diag[:, :, :], ident[0:NS, 0:NS].unsqueeze(2).broadcast_to([NS, NS, NK]),
                                    att[:, :].unsqueeze(1).broadcast_to([NS, NS, NK]), ALU.mult).then_inc(soft, 1)

            def finish_table():
                dve.wait_ge(att_mm, 1)
                nc.vector.tensor_copy(table[:, :, 0:NK], ps[:, 7, :].rearrange("p (s k) -> p s k", k=NK)
                                      ).then_inc(table_made, 1)
                dve.wait_ge(table_made, 2)
                nc.vector.tensor_tensor(aggb_prod, table[:, :, 0:NK],
                                        mixb_t[:, :].unsqueeze(1).broadcast_to([P, NS, NK]),
                                        ALU.mult).then_inc(table_made, 1)
                dve.wait_ge(table_made, 3)
                nc.vector.tensor_reduce(table[:, :, NK + 1:NK + 2].rearrange("p s a -> p (s a)"), aggb_prod,
                                        AX.X, ALU.add).then_inc(table_made, 1)

            def slot(s):
                split_y(after(s, -1))
                if is_sample(s, 0):
                    finish_table()
                else:
                    split_x(after(s, 1))
                take_y(s)

            pipeline(dve, slot)

        @block.gpsimd
        def _(pool):
            nc.gpsimd.memset(ident[:, :], 0.0).then_inc(ident_made, 1)
            pool.wait_ge(ident_made, 1)
            nc.gpsimd.affine_select(out=ident[:, :], in_=ident[:, :], compare_op=ALU.not_equal, fill=1.0,
                                    base=0, pattern=[[-1, P]], channel_multiplier=1).then_inc(ident_made, 1)
            nc.gpsimd.memset(cw_f[:, :, :, :], 0.0).then_inc(cw_cleared, 1)
            for part in (x_hi, x_lo):
                for k in range(2):
                    nc.gpsimd.memset(part[k][:, :, 0:N + 2:N + 1].bitcast(F32), 0.0).then_inc(halos_cleared, 1)
            nc.gpsimd.memset(ones[:, :], 1.0).then_inc(consts_made, 1)
            pool.wait_ge(ident_made, 2)
            pool.wait_ge(cw_cleared, 1)
            pool.wait_ge(halos_cleared, 4)
            pool.wait_ge(consts_made, 1)
            pool.wait_ge(x_loaded[0], DMA)
            g = G - 1
            for p in range(PH):
                nc.gpsimd.tensor_copy(
                    x_cv[0][Q * p:Q * p + Q, g, 0, :],
                    x_in[0][Q * g:Q * g + Q, :].rearrange("c (n q) -> c q n", q=PH)[:, p, :]
                ).then_inc(x0_by_pool, 1)
                pool.wait_ge(x0_by_pool, p + 1)
            pool.wait_ge(x_split_ph, 2)
            for p in range(PH):
                last = p == PH - 1
                nc.gpsimd.tensor_copy(x_cv[0][Q * p:Q * p + Q, g, 1, :], x_ph[0][Q * g:Q * g + Q, p, 1, :]).then_inc(
                    x_moved[0] if last else x1_by_pool, DMA * PH if last else 1)
                if not last:
                    pool.wait_ge(x1_by_pool, p + 1)
            pool.wait_ge(x_moved[0], DMA * PH * G)

            def mix_matrix(s):
                if not exists(s):
                    return
                at_least(pool, z_read, done(s, lag=-2))
                pool.wait_ge(table_made, 4)
                nc.gpsimd.tensor_copy(par[buf(s)][:, :], table[:, number(s), :]).then_inc(par_made, 1)
                pool.wait_ge(par_made, done(s))
                for k in range(0, NK, NK // 2):
                    ks = slice(k, k + NK // 2)
                    nc.gpsimd.tensor_tensor(mix_prod[:, ks, :], mixw_t[:, ks, :],
                                            par[buf(s)][:, ks].unsqueeze(2).broadcast_to([P, NK // 2, P]),
                                            ALU.mult).then_inc(prod_made, 1)
                pool.wait_ge(prod_made, done(s, 2))
                for n, half in enumerate((4, 2)):
                    nc.gpsimd.tensor_tensor(mix_prod[:, 0:half, :], mix_prod[:, 0:half, :],
                                            mix_prod[:, half:2 * half, :], ALU.add).then_inc(mix_sum, 1)
                    pool.wait_ge(mix_sum, done(s, 3, lag=-1) + n + 1)
                nc.gpsimd.tensor_tensor(mix_sum_f[:, :], mix_prod[:, 0, :], mix_prod[:, 1, :],
                                        ALU.add).then_inc(mix_sum, 1)
                pool.wait_ge(mix_sum, done(s, 3))
                nc.gpsimd.tensor_tensor(mix_f[:, :], mix_sum_f[:, :], ident[:, :], ALU.add)
                nc.gpsimd.tensor_tensor(mix_hi[buf(s)][:, :], mix_sum_f[:, :], ident[:, :],
                                        ALU.add).then_inc(mix_hi_made, 1)
                pool.wait_ge(mix_hi_made, done(s))
                nc.gpsimd.tensor_tensor(mix_lo[buf(s)][:, :], mix_f[:, :], mix_hi[buf(s)][:, :].bitcast(F32),
                                        ALU.subtract).then_inc(mix_made, 1)
                pool.wait_ge(mix_made, done(s))

            pool.wait_ge(table_made, 4)
            pool.wait_ge(mixw_copied, 1)
            pipeline(pool, mix_matrix)


_INS = ["x", "cond_128", "fside_S_0", "L0_cond_weight", "L0_cond_c_weight", "L1_cond_W0", "L1_cond_b0",
        "L1_cond_W1", "L1_cond_b1", "L1_cond_W2", "L1_cond_b2", "L1_cond_weight", "L1_cond_bias_k"]


def kernel(**inputs):
    import numpy as np
    import concourse.bacc as bacc
    from concourse.bass_utils import run_bass_kernel_spmd

    nc = bacc.Bacc("TRN2", target_bir_lowering=False, num_devices=1)
    arrays, args = {}, []
    for name in _INS:
        a = np.ascontiguousarray(inputs[name])
        arrays[f"in_{name}_dram"] = a
        args.append(nc.dram_tensor(f"in_{name}_dram", a.shape, mybir.dt.from_np(a.dtype), kind="ExternalInput").ap())
    shape = inputs["x"].shape
    args.append(nc.dram_tensor("out_dram", shape, F32, kind="ExternalOutput").ap())
    cond_resid_kernel(nc, *args)
    r = run_bass_kernel_spmd(nc, [arrays], core_ids=[0])
    return r.results[0]["out_dram"]
```
